# Optimizing a Trainium2 kernel written in Bass

```python
import numpy as np
import jax
import jax.numpy as jnp

def _softmax(x, axis=-1):
    return jax.nn.softmax(x, axis=axis)

def _gelu(x):
    return jax.nn.gelu(x, approximate=True)

def _silu(x):
    return jax.nn.silu(x)

def _sigmoid(x):
    return jax.nn.sigmoid(x)

def _layernorm(x, axis=-1, eps=1e-05):
    m = jnp.mean(x, axis=axis, keepdims=True)
    v = jnp.var(x, axis=axis, keepdims=True)
    return (x - m) / jnp.sqrt(v + eps)

def _scatter_add(tgt, idx, src, axis=0):
    return tgt.at[idx].add(src)

def _segment_sum(src, seg, n):
    return jax.ops.segment_sum(src, seg, n)
kernel_name = 'mk_adaln_ffn_d1_seqx_r2_3c370b'

def setup_inputs(seed: int=0):
    np.random.seed(seed)
    _w = jnp.asarray

    def _rec_inputs():
        import jax
        import jax.numpy as jnp
        _rk = jax.random.key(seed)
        x = -0.0003929 + 0.9999 * jax.random.normal(jax.random.fold_in(_rk, 1), (128, 128, 512), jnp.float32)
        _lenS = 128 - jax.random.randint(jax.random.fold_in(_rk, 7), (128,), 0, max(1, 128 // 4) + 1, jnp.int32)
        _lenS2 = 128 - jax.random.randint(jax.random.fold_in(_rk, 8), (128,), 0, max(1, 128 // 4) + 1, jnp.int32)
        itok_B_0_63 = jax.random.randint(jax.random.fold_in(_rk, 11), (128,), 0, 64, jnp.int32)
        return (x, itok_B_0_63)
    x, itok_B_0_63 = _rec_inputs()

    def _L0_cond_setup():
        import jax, jax.numpy as jnp
        import numpy as np
        NUM_CATEGORIES = 64
        INPUT_DIM = 512
        HIDDEN_DIM = 512
        B = 128
        S = 64
        key = jax.random.key(seed)
        kx, kc, kw = jax.random.split(key, 3)
        x = jax.random.normal(kx, (B, S, INPUT_DIM), dtype=jnp.float32)
        cat_ids = jax.random.randint(kc, (B,), 0, NUM_CATEGORIES, dtype=jnp.int32)
        W = 0.02 * jax.random.normal(kw, (NUM_CATEGORIES, INPUT_DIM, HIDDEN_DIM), dtype=jnp.float32)
        b = jnp.zeros((NUM_CATEGORIES, HIDDEN_DIM), dtype=jnp.float32)
        return {'x': x, 'cat_ids': cat_ids, 'W': W, 'b': b}
    _L0_cond_all = _L0_cond_setup()
    _L0_cond_in = {k: v for k, v in _L0_cond_all.items() if k in ('W', 'b')}
    del _L0_cond_all

    def _L0_ffn_setup():
        import jax, jax.numpy as jnp
        import numpy as np
        EPS = 1e-08
        key = jax.random.key(seed)
        kx, kw = jax.random.split(key)
        x = jax.random.normal(kx, (8, 2048, 512), dtype=jnp.float32)
        weight = jax.random.normal(kw, (512, 512), dtype=jnp.float32) * (1.0 / np.sqrt(512))
        return {'x': x, 'weight': weight}
    _L0_ffn_all = _L0_ffn_setup()
    _L0_ffn_in = {k: v for k, v in _L0_ffn_all.items() if k in ('weight',)}
    del _L0_ffn_all
    return {'x': x, 'itok_B_0_63': itok_B_0_63, 'L0_cond_W': _L0_cond_in['W'], 'L0_cond_b': _L0_cond_in['b'], 'L0_ffn_weight': _L0_ffn_in['weight']}

def reference(x, itok_B_0_63, L0_cond_W, L0_cond_b, L0_ffn_weight):
    import jax
    import jax.numpy as jnp

    def _L0_cond_ref(x, cat_ids, W, b):
        import jax, jax.numpy as jnp
        import numpy as np
        NUM_CATEGORIES = 64
        INPUT_DIM = 512
        HIDDEN_DIM = 512
        B = 128
        S = 64
        selected_W = W[cat_ids]
        selected_b = b[cat_ids]
        out = jnp.einsum('bsd,bdh->bsh', x, selected_W) + selected_b[:, None, :]
        return out

    def _L0_ffn_ref(x, weight):
        import jax, jax.numpy as jnp
        import numpy as np
        EPS = 1e-08
        w_scale = jnp.mean(jnp.abs(weight)) + EPS
        u = weight / w_scale
        w_quant = u + jax.lax.stop_gradient(jnp.clip(jnp.round(u), -1.0, 1.0) - u)
        a_scale = jnp.max(jnp.abs(x), axis=-1, keepdims=True) + EPS
        z = jnp.clip(x / a_scale * 127.0, -128.0, 127.0)
        a_quant = z + jax.lax.stop_gradient(jnp.round(z) - z)
        y = jnp.einsum('bsi,oi->bso', a_quant, w_quant)
        y = y * (w_scale * a_scale / 127.0)
        return y
    x = x + _L0_ffn_ref(_L0_cond_ref(x, itok_B_0_63, L0_cond_W, L0_cond_b), L0_ffn_weight)
    return x

_drawn_inputs = setup_inputs


def setup_inputs(seed=0):
    import zlib

    import numpy as np

    out = dict(_drawn_inputs(seed))
    spreads = {'L0_cond_b': (0.0, 0.1)}
    factors = {}
    for name, (base, spread) in spreads.items():
        noise = np.random.default_rng([zlib.crc32(name.encode()), seed]).standard_normal(out[name].shape)
        drawn = base * np.exp(spread * noise) if base else spread * noise
        out[name] = jnp.asarray(drawn.astype(out[name].dtype))
    for name, factor in factors.items():
        out[name] = (out[name] * factor).astype(out[name].dtype)
    return out
```

```python
import concourse.bass as bass
from concourse import mybir
from contextlib import ExitStack

F32 = mybir.dt.float32
F32R = mybir.dt.float32r
BF16 = mybir.dt.bfloat16
I32 = mybir.dt.int32
ALU = mybir.AluOpType
ACT = mybir.ActivationFunctionType
AX = mybir.AxisListType

P = 128
EPS = 1e-8
LEVELS = 127.0
ROUNDER = 1.5 * 2.0**23

NEW, W_OFFSET, BIAS_OFFSET, CATEGORY, COLUMNS = 0, 1, 2, 3, 4


def adaln_ffn(nc, x, itok, cond_w, cond_b, ffn_w, out):
    B, S, D = x.shape
    C, _, H = cond_w.shape
    O = ffn_w.shape[0]
    assert B == P and S == P and ffn_w.shape[1] == H and O == D
    KD, KH, KO = D // P, H // P, O // P

    U = 8
    W_RING, BIAS_RING, XT_RING, OUT_RING, Q_RING, PS_RING, STAT_RING = 4, 8, 4, 4, 2, 2, 4
    W_AHEAD, X_AHEAD, MM2_BEHIND = 3, 2, 2
    W_FREE = KD * H
    QUARTER = W_FREE // 4
    POOL_COLUMNS = W_FREE // 2

    ctx = ExitStack()
    with ctx:
        def sb(name, shape, dt=F32):
            return ctx.enter_context(nc.sbuf_tensor("sb_" + name, shape, dt))

        def sem(name):
            return ctx.enter_context(nc.semaphore(name))

        w_raw = sb("w_raw", [P, W_RING * W_FREE])
        w_hi = sb("w_hi", [P, W_RING * W_FREE], F32R)
        w_lo = sb("w_lo", [P, W_RING * W_FREE], F32R)
        bias = sb("bias", [P, BIAS_RING * H])
        x_in = sb("x_in", [P, U, D])
        xT_hi = sb("xT_hi", [P, XT_RING, D], F32R)
        xT_lo = sb("xT_lo", [P, XT_RING, D], F32R)
        cond = sb("cond", [P, Q_RING, H])
        a_rounded = sb("a_rounded", [P, Q_RING, H])
        a_int = sb("a_int", [P, Q_RING, H], BF16)
        aT = sb("aT", [P, Q_RING, H], BF16)
        y_out = sb("y_out", [P, OUT_RING, O])
        absmax = sb("absmax", [P, STAT_RING])
        a_step = sb("a_step", [P, STAT_RING])
        a_inv = sb("a_inv", [P, STAT_RING])
        y_scale = sb("y_scale", [P, STAT_RING])

        ident = sb("ident", [P, P])
        ident_bf = sb("ident_bf", [P, P], BF16)
        ones = sb("ones", [P, P])
        rounder = sb("rounder", [P, 1])
        free_index = sb("free_index", [P, P])
        part_index = sb("part_index", [P, 1])
        cat_row_i = sb("cat_row_i", [P, B], I32)
        cat_col_i = sb("cat_col_i", [P, 1], I32)
        cat_row = sb("cat_row", [P, B])
        cat_col = sb("cat_col", [P, 1])
        key_row = sb("key_row", [P, B])
        key_col = sb("key_col", [P, 1])
        key_below = sb("key_below", [P, B])
        cat_below = sb("cat_below", [P, B])
        n_below = sb("n_below", [P, 1])
        rank = sb("rank", [P, 1])
        is_first = sb("is_first", [P, 1], BF16)
        later_cat = sb("later_cat", [P, B], BF16)
        place = sb("place", [P, B], BF16)
        cat_col_bf = sb("cat_col_bf", [P, 1], BF16)
        part_index_bf = sb("part_index_bf", [P, 1], BF16)
        n_cats_below = sb("n_cats_below", [P, 1], I32)
        slots = sb("slots", [P, 2], I32)
        w_offset_col = sb("w_offset_col", [P, 1], BF16)
        bias_offset_col = sb("bias_offset_col", [P, 1], BF16)
        table = sb("table", [1, B, COLUMNS], I32)
        element_table = sb("element_table", [1, B], I32)
        ffn_abs = sb("ffn_abs", [P, KO * H], BF16)
        ffn_raw = sb("ffn_raw", [P, KO, H])
        ffn_sum = sb("ffn_sum", [P, 1])
        w_scale = sb("w_scale", [P, 1])
        w_inv = sb("w_inv", [P, 1])
        ffn_plus = sb("ffn_plus", [P, KO, H], BF16)
        ffn_minus = sb("ffn_minus", [P, KO, H], BF16)
        ffn_tern = sb("ffn_tern", [P, KO, H], BF16)
        ffnT = sb("ffnT", [P, KH, O], BF16)
        marks = sb("marks", [P, 3])

        def ps(name, dt=F32):
            return ctx.enter_context(nc.psum_tensor("ps_" + name, [P, 512], dt))

        xT_ps = [ps(f"xT{n}") for n in range(PS_RING)]
        cond_ps = [ps(f"cond{n}") for n in range(PS_RING)]
        y_ps = [ps(f"y{n}") for n in range(PS_RING)]
        aT_ps = [ctx.enter_context(nc.psum_tensor(f"ps_aT{n}", [P, 1024], BF16)) for n in range(PS_RING)]

        ids_loaded = sem("ids_loaded")
        ffn_loaded = sem("ffn_loaded")
        x_loaded = [sem(f"x_loaded{n}") for n in range(U)]
        w_loaded = [sem(f"w_loaded{n}") for n in range(U)]
        stored = [sem(f"stored{n}") for n in range(OUT_RING)]
        consts_done = sem("consts_done")
        start_dve = sem("start_dve")
        placed = sem("placed")
        offsets_there = sem("offsets_there")
        ffn_summed = sem("ffn_summed")
        ffn_ternary = sem("ffn_ternary")
        table_done = sem("table_done")
        elements_done = sem("elements_done")
        counts_mm_done = sem("counts_mm_done")
        elements_mm_done = sem("elements_mm_done")
        table_mm_done = sem("table_mm_done")
        ffn_sum_mm_done = sem("ffn_sum_mm_done")
        ffn_T_done = sem("ffn_T_done")
        ffn_T_moved = sem("ffn_T_moved")
        start_hi_done = sem("start_hi_done")
        start_lo_done = sem("start_lo_done")
        pool_w_done = sem("pool_w_done")
        xT_done = sem("xT_done")
        x_hi_done = sem("x_hi_done")
        x_lo_done = sem("x_lo_done")
        cond_mm_done = sem("cond_mm_done")
        cond_done = sem("cond_done")
        absmax_done = sem("absmax_done")
        a_step_done = sem("a_step_done")
        a_inv_done = sem("a_inv_done")
        y_scale_done = sem("y_scale_done")
        a_rounded_done = sem("a_rounded_done")
        a_taken = sem("a_taken")
        a_int_done = sem("a_int_done")
        aT_done = sem("aT_done")
        aT_moved = sem("aT_moved")
        y_mm_done = sem("y_mm_done")
        y_done = sem("y_done")

        cond_w_v = cond_w.rearrange("c (k p) h -> c p k h", p=P)
        block = ctx.enter_context(nc.Block())

        def row_of(eng, step, first, n):
            _, values = nc.values_load_multi_w_load_instructions(
                table[0:1, bass.ds(step, 1), first:first + n].rearrange("a s c -> a (s c)"),
                engines=[eng.engine], skip_runtime_bounds_check_because=
                "the table's entries are clamped or ranks among 128 when it is computed")
            return values

        def bounded(eng, value, most):
            return nc.s_assert_within(value, 0, most, skip_runtime_bounds_check_because=
                                      "the table's entries are clamped categories, ranks and slots")

        def element_of(eng, step):
            _, (element,) = nc.values_load_multi_w_load_instructions(
                element_table[0:1, bass.ds(step, 1)], engines=[eng.engine],
                skip_runtime_bounds_check_because="the elements of the table are ranks among 128")
            return bounded(eng, element, B - 1)

        def w_slot(eng, step):
            new, offset = row_of(eng, step, NEW, 2)
            return bounded(eng, new, 1), bounded(eng, offset, (W_RING - 1) * W_FREE)

        def over_steps(eng, body):
            for u in range(U):
                body(0, u, True, False)
            with eng.Fori(1, B // U - 1) as group:
                r0 = eng.snap(group * U)
                for u in range(U):
                    body(r0, u, False, False)
            for u in range(U):
                body(B - U, u, False, True)

        @block.sync
        def _(sp):
            sp.dma_start(cat_row_i[:, :], itok.rearrange("(a b) -> a b", a=1).to_broadcast([P, B])).then_inc(ids_loaded, 16)
            sp.dma_start(cat_col_i[:, :], itok.rearrange("(p a) -> p a", a=1)).then_inc(ids_loaded, 16)
            sp.dma_start(ffn_raw[:, :, :], ffn_w.rearrange("(k p) h -> p k h", p=P)).then_inc(ffn_loaded, 16)
            sp.wait_ge(elements_done, 1)

            def store(step, u):
                element = element_of(sp, step)
                sp.dma_start(out[bass.ds(element, 1), :, :].rearrange("a s o -> (a s) o"),
                             y_out[:, u % OUT_RING, :]).then_inc(stored[u % OUT_RING], 16)

            def load_x(step, u):
                element = element_of(sp, step)
                sp.dma_start(x_in[:, u, :],
                             x[bass.ds(element, 1), :, :].rearrange("a s d -> (a s) d")).then_inc(x_loaded[u], 16)

            load_x(0, 0)
            load_x(1, 1)
            sp.wait_ge(table_done, 1)

            def body(r0, u, first, last):
                r = r0 + u
                if not first:
                    sp.wait_ge(y_done, r - (U - 1))
                    store(r - U, u)
                new, w_offset, bias_offset, category = row_of(sp, r, NEW, 4)
                new = bounded(sp, new, 1)
                w_offset = bounded(sp, w_offset, (W_RING - 1) * W_FREE)
                bias_offset = bounded(sp, bias_offset, (BIAS_RING - 1) * H)
                category = bounded(sp, category, C - 1)
                with sp.If(new > 0):
                    if first and u >= W_RING:
                        if u - W_RING < W_AHEAD:
                            sp.wait_ge(start_lo_done, min(u - W_RING + 1, 2))
                            sp.wait_ge(pool_w_done, min(u - W_RING + 1, 2))
                        else:
                            sp.wait_ge(cond_done, u - W_RING - W_AHEAD + 2)
                    if not first or u - W_RING >= W_AHEAD:
                        sp.wait_ge(a_int_done, r - W_RING - W_AHEAD + 2)
                    sp.dma_start(
                        w_raw[:, bass.ds(w_offset, W_FREE)].rearrange("p (k h) -> p k h", k=KD),
                        cond_w_v[bass.ds(category, 1), :, :, :].rearrange("c p k h -> (c p) k h"),
                    ).then_inc(w_loaded[u], 16)
                    sp.dma_start(bias[:, bass.ds(bias_offset, H)],
                                 cond_b[bass.ds(category, 1), :].to_broadcast([P, H])).then_inc(w_loaded[u], 16)
                with sp.Else():
                    sp.sem_inc(w_loaded[u], 32)
                if not first or u >= 2:
                    load_x(r, u)

            over_steps(sp, body)
            for u in range(U):
                sp.wait_ge(y_done, B - U + u + 1)
                store(B - U + u, u)
            for n in range(OUT_RING):
                sp.wait_ge(stored[n], 16 * (B // OUT_RING))

        @block.gpsimd
        def _(pool):
            pool.memset(ident[:, :], 1.0).then_inc(consts_done, 1)
            pool.memset(ones[:, :], 1.0).then_inc(consts_done, 1)
            pool.memset(rounder[:, :], ROUNDER).then_inc(consts_done, 1)
            pool.iota(free_index[:, :], [[1, P]], base=0, channel_multiplier=0,
                      allow_small_or_imprecise_dtypes=True).then_inc(consts_done, 1)
            pool.iota(part_index[:, :], [[1, 1]], base=0, channel_multiplier=1,
                      allow_small_or_imprecise_dtypes=True).then_inc(consts_done, 1)
            pool.wait_ge(consts_done, 5)
            pool.affine_select(out=ident[:, :], in_=ident[:, :], compare_op=ALU.is_equal, fill=0.0,
                               base=0, pattern=[[-1, P]], channel_multiplier=1).then_inc(consts_done, 1)

            def w_low(offset, n=POOL_COLUMNS):
                return pool.tensor_tensor(w_lo[:, bass.ds(offset, n)], w_raw[:, bass.ds(offset, n)],
                                          w_hi[:, bass.ds(offset, n)].bitcast(F32), ALU.subtract)

            pool.wait_ge(table_done, 1)
            pool.wait_ge(start_hi_done, 1)
            w_low(0, QUARTER).then_inc(pool_w_done, 1)
            pool.wait_ge(start_hi_done, 3)
            for step in (1, 2):
                new, offset = w_slot(pool, step)
                with pool.If(new > 0):
                    w_low(offset)
            pool.memset(marks[:, 0:1], 0.0).then_inc(pool_w_done, 1)

            def body(r0, u, first, last):
                r = r0 + u
                pool.wait_ge(a_rounded_done, r + 1)
                pool.sem_inc(a_taken, 1)
                pool.tensor_scalar(a_int[:, u % Q_RING, :], a_rounded[:, u % Q_RING, :],
                                   -ROUNDER, 1.0, ALU.add, ALU.mult).then_inc(a_int_done, 1)
                if not last or u + W_AHEAD < U:
                    new, offset = w_slot(pool, r + W_AHEAD)
                    with pool.If(new > 0):
                        pool.wait_ge(x_hi_done, r + X_AHEAD + 1)
                        w_low(offset)

            over_steps(pool, body)

        @block.scalar
        def _(act):
            def w_high(offset, n=W_FREE):
                return act.activation(w_hi[:, bass.ds(offset, n)], w_raw[:, bass.ds(offset, n)], ACT.Copy)

            def x_high(step, u):
                act.wait_ge(xT_done, step + 1)
                act.activation(xT_hi[:, u % XT_RING, :], xT_ps[u % PS_RING][:, :], ACT.Copy).then_inc(x_hi_done, 1)

            act.wait_ge(consts_done, 3)
            act.activation(marks[:, 1:2], rounder[:, :], ACT.Abs)
            act.wait_ge(elements_mm_done, 1)
            act.activation(element_table[:, :], y_ps[1][0:1, 0:B], ACT.Copy).then_inc(elements_done, 1)
            act.wait_ge(ffn_loaded, 16)
            act.activation(ffn_abs[:, :], ffn_raw[:, :, :].rearrange("p k h -> p (k h)"), ACT.Abs,
                           accum_out=ffn_sum[:, 0:1]).then_inc(ffn_summed, 1)
            x_high(0, 0)
            x_high(1, 1)
            act.wait_ge(w_loaded[0], 32)
            for at in (0, QUARTER):
                w_high(at, QUARTER).then_inc(start_hi_done, 1)
            half = KH // PS_RING
            for n in range(PS_RING):
                act.wait_ge(ffn_T_done, n + 1)
                act.activation(ffnT[:, n * half:(n + 1) * half, :].rearrange("p k o -> p (k o)"),
                               aT_ps[n][:, 0:half * O], ACT.Copy).then_inc(ffn_T_moved, 1)
            act.wait_ge(table_done, 1)
            for step in (1, 2):
                new, offset = w_slot(act, step)
                with act.If(new > 0):
                    act.wait_ge(w_loaded[step], 32)
                    w_high(offset)
            act.activation(marks[:, 1:2], rounder[:, :], ACT.Copy).then_inc(start_hi_done, 1)

            def body(r0, u, first, last):
                r = r0 + u
                if not last or u + W_AHEAD < U:
                    new, offset = w_slot(act, r + W_AHEAD)
                    n = (u + W_AHEAD) % U
                    with act.If(new > 0):
                        act.wait_ge(w_loaded[n], (r + W_AHEAD - n) * (32 // U) + 32)
                        if not first or u:
                            act.wait_ge(cond_mm_done, r)
                        w_high(offset)
                if not last or u + X_AHEAD < U:
                    if not first or u >= XT_RING - X_AHEAD:
                        act.wait_ge(cond_mm_done, r + X_AHEAD - XT_RING + 1)
                    x_high(r + X_AHEAD, (u + X_AHEAD) % U)

                def move(step, u):
                    act.wait_ge(aT_done, step + 1)
                    if not first or u >= Q_RING:
                        act.wait_ge(y_mm_done, step - Q_RING + 1)
                    act.activation(aT[:, u % Q_RING, :], aT_ps[u % PS_RING][:, 0:H], ACT.Copy).then_inc(aT_moved, 1)

                if not first or u:
                    move(r - 1, (u - 1) % U)
                if not first or u >= Q_RING:
                    act.wait_ge(a_int_done, r - Q_RING + 1)
                act.wait_ge(a_inv_done, r + 1)
                act.activation(a_rounded[:, u % Q_RING, :], cond[:, u % Q_RING, :], ACT.Identity,
                               bias=rounder[:, 0:1], scale=a_inv[:, u % STAT_RING:u % STAT_RING + 1]).then_inc(a_rounded_done, 1)
                if last and u == U - 1:
                    move(r, u)

            over_steps(act, body)

        @block.vector
        def _(dve):
            begun = [0]

            def begin(instruction):
                begun[0] += 1
                instruction.then_inc(start_dve, 1)

            def done():
                dve.wait_ge(start_dve, begun[0])

            dve.wait_ge(ids_loaded, 32)
            begin(dve.tensor_scalar(cat_col[:, :], cat_col_i[:, :], 0.0, float(C - 1), ALU.max, ALU.min))
            begin(dve.tensor_scalar(cat_row[:, :], cat_row_i[:, :], 0.0, float(C - 1), ALU.max, ALU.min))
            dve.wait_ge(consts_done, 6)
            done()
            begin(dve.scalar_tensor_tensor(key_col[:, :], cat_col[:, :], float(B), part_index[:, :], ALU.mult, ALU.add))
            begin(dve.scalar_tensor_tensor(key_row[:, :], cat_row[:, :], float(B), free_index[:, :], ALU.mult, ALU.add))
            begin(dve.tensor_scalar(cat_below[:, :], cat_row[:, :], cat_col[:, 0:1], None, ALU.is_lt))
            begin(dve.tensor_scalar(later_cat[:, :], cat_row[:, :], cat_col[:, 0:1], None, ALU.is_gt))
            done()
            begin(dve.tensor_copy(cat_col_bf[:, :], cat_col[:, :]))
            begin(dve.tensor_copy(part_index_bf[:, :], part_index[:, :]))
            begin(dve.tensor_scalar(key_below[:, :], key_row[:, :], key_col[:, 0:1], None, ALU.is_lt))
            begin(dve.tensor_reduce(n_below[:, :], cat_below[:, :], AX.X, ALU.add))
            done()
            begin(dve.tensor_reduce(rank[:, :], key_below[:, :], AX.X, ALU.add))
            done()
            begin(dve.tensor_tensor(is_first[:, :], rank[:, :], n_below[:, :], ALU.is_equal))
            dve.tensor_scalar(place[:, :], free_index[:, :], rank[:, 0:1], None, ALU.is_equal).then_inc(placed, 1)
            dve.wait_ge(counts_mm_done, 1)
            begin(dve.tensor_copy(n_cats_below[:, :], xT_ps[0][:, 0:1]))
            done()
            begin(dve.tensor_scalar(slots[:, 0:1], n_cats_below[:, :], W_RING - 1, None, ALU.bitwise_and))
            begin(dve.tensor_scalar(slots[:, 1:2], n_cats_below[:, :], BIAS_RING - 1, None, ALU.bitwise_and))
            done()
            begin(dve.tensor_scalar(w_offset_col[:, :], slots[:, 0:1], float(W_FREE), None, ALU.mult))
            dve.tensor_scalar(bias_offset_col[:, :], slots[:, 1:2], float(H), None, ALU.mult).then_inc(offsets_there, 1)
            begin(dve.tensor_copy(ident_bf[:, :], ident[:, :]))
            dve.wait_ge(table_mm_done, 1)
            dve.tensor_copy(table[:, :, :].rearrange("a b c -> a (b c)"), cond_ps[0][0:1, :]).then_inc(table_done, 1)

            dve.wait_ge(ffn_sum_mm_done, 1)
            begin(dve.tensor_scalar(w_scale[:, :], y_ps[0][:, 0:1], 1.0 / (O * H), EPS, ALU.mult, ALU.add))
            done()
            begin(dve.reciprocal(w_inv[:, :], w_scale[:, :]))
            done()
            begin(dve.tensor_scalar(ffn_plus[:, :, :], ffn_raw[:, :, :], w_inv[:, 0:1], 0.5, ALU.mult, ALU.is_gt))
            begin(dve.tensor_scalar(ffn_minus[:, :, :], ffn_raw[:, :, :], w_inv[:, 0:1], -0.5, ALU.mult, ALU.is_lt))
            done()
            dve.tensor_tensor(ffn_tern[:, :, :], ffn_plus[:, :, :], ffn_minus[:, :, :], ALU.subtract).then_inc(ffn_ternary, 1)

            def w_low(offset, at=POOL_COLUMNS, n=W_FREE - POOL_COLUMNS):
                at = offset + at
                return dve.tensor_tensor(w_lo[:, bass.ds(at, n)], w_raw[:, bass.ds(at, n)],
                                         w_hi[:, bass.ds(at, n)].bitcast(F32), ALU.subtract)

            def x_low(step, u):
                dve.wait_ge(x_hi_done, step + 1)
                n = u % XT_RING
                dve.tensor_tensor(xT_lo[:, n, :], xT_ps[u % PS_RING][:, :], xT_hi[:, n, :].bitcast(F32),
                                  ALU.subtract).then_inc(x_lo_done, 1)

            x_low(0, 0)
            x_low(1, 1)
            dve.wait_ge(w_loaded[0], 32)
            begin(dve.tensor_copy(w_hi[:, 2 * QUARTER:W_FREE], w_raw[:, 2 * QUARTER:W_FREE]))
            done()
            w_low(0, 2 * QUARTER, 2 * QUARTER)
            dve.wait_ge(start_hi_done, 2)
            w_low(0, QUARTER, QUARTER).then_inc(start_lo_done, 1)
            dve.wait_ge(start_hi_done, 3)
            for step in (1, 2):
                new, offset = w_slot(dve, step)
                with dve.If(new > 0):
                    w_low(offset)
            dve.memset(marks[:, 2:3], 0.0).then_inc(start_lo_done, 1)

            def result(step, u, first):
                dve.wait_ge(y_mm_done, step + 1)
                dve.wait_ge(y_scale_done, step + 1)
                if not first or u >= OUT_RING:
                    dve.wait_ge(stored[u % OUT_RING], (step - u % OUT_RING) * (16 // OUT_RING))
                dve.scalar_tensor_tensor(y_out[:, u % OUT_RING, :], y_ps[u % PS_RING][:, :],
                                         y_scale[:, u % STAT_RING:u % STAT_RING + 1], x_in[:, u, :],
                                         ALU.mult, ALU.add).then_inc(y_done, 1)

            def body(r0, u, first, last):
                r = r0 + u
                q, s = u % Q_RING, u % STAT_RING
                (bias_offset,) = row_of(dve, r, BIAS_OFFSET, 1)
                bias_offset = bounded(dve, bias_offset, (BIAS_RING - 1) * H)
                if not last or u + W_AHEAD < U:
                    new, w_offset = w_slot(dve, r + W_AHEAD)
                dve.wait_ge(cond_mm_done, r + 1)
                if not first or u >= Q_RING:
                    dve.wait_ge(a_rounded_done, r - Q_RING + 1)
                dve.tensor_tensor(cond[:, q, :], cond_ps[u % PS_RING][:, :], bias[:, bass.ds(bias_offset, H)],
                                  ALU.add).then_inc(cond_done, 1)
                dve.wait_ge(cond_done, r + 1)
                dve.tensor_reduce(absmax[:, s:s + 1], cond[:, q, :], AX.X, ALU.max,
                                  apply_absolute_value=True).then_inc(absmax_done, 1)
                dve.wait_ge(absmax_done, r + 1)
                dve.tensor_scalar(a_step[:, s:s + 1], absmax[:, s:s + 1], EPS, 1.0 / LEVELS,
                                  ALU.add, ALU.mult).then_inc(a_step_done, 1)
                dve.wait_ge(a_step_done, r + 1)
                dve.reciprocal(a_inv[:, s:s + 1], a_step[:, s:s + 1]).then_inc(a_inv_done, 1)
                dve.tensor_tensor(y_scale[:, s:s + 1], a_step[:, s:s + 1], w_scale[:, :],
                                  ALU.mult).then_inc(y_scale_done, 1)
                if not last or u + X_AHEAD < U:
                    x_low(r + X_AHEAD, (u + X_AHEAD) % U)
                if not last or u + W_AHEAD < U:
                    with dve.If(new > 0):
                        dve.wait_ge(x_hi_done, r + X_AHEAD + 1)
                        w_low(w_offset)
                if not first or u >= MM2_BEHIND:
                    result(r - MM2_BEHIND, (u - MM2_BEHIND) % U, first)

            over_steps(dve, body)
            for u in range(U - MM2_BEHIND, U):
                result(B - U + u, u, False)

        @block.tensor
        def _(pe):
            pe.wait_ge(placed, 1)
            pe.matmul(xT_ps[0][:, 0:1], later_cat[:, :], is_first[:, :], start=True, stop=True).then_inc(counts_mm_done, 1)
            pe.matmul(y_ps[1][0:1, 0:B], part_index_bf[:, 0:1], place[:, :], start=True, stop=True).then_inc(elements_mm_done, 1)
            table_ps = cond_ps[0][0:1, :].rearrange("a (b c) -> a b c", c=COLUMNS)
            pe.matmul(table_ps[:, :, NEW], is_first[:, 0:1], place[:, :], start=True, stop=False, skip_group_check=True)
            pe.matmul(table_ps[:, :, CATEGORY], cat_col_bf[:, 0:1], place[:, :], start=False, stop=False, skip_group_check=True)
            pe.wait_ge(offsets_there, 1)
            pe.matmul(table_ps[:, :, W_OFFSET], w_offset_col[:, 0:1], place[:, :], start=False, stop=False, skip_group_check=True)
            pe.matmul(table_ps[:, :, BIAS_OFFSET], bias_offset_col[:, 0:1], place[:, :], start=False, stop=True,
                      skip_group_check=True).then_inc(table_mm_done, 1)

            def x_transpose(step, u):
                pe.wait_ge(x_loaded[u], (step - u) * (16 // U) + 16)
                for k in range(KD):
                    last = pe.transpose(xT_ps[u % PS_RING][:, k * P:(k + 1) * P], x_in[:, u, k * P:(k + 1) * P], ident[:, :])
                last.then_inc(xT_done, 1)

            pe.wait_ge(ffn_summed, 1)
            pe.matmul(y_ps[0][:, 0:1], ones[:, :], ffn_sum[:, :], start=True, stop=True).then_inc(ffn_sum_mm_done, 1)
            x_transpose(0, 0)
            x_transpose(1, 1)
            pe.wait_ge(ffn_ternary, 1)
            half = KH // PS_RING
            for k in range(KH):
                for o in range(KO):
                    at = (k % half) * O + o * P
                    last = pe.transpose(aT_ps[k // half][:, at:at + P],
                                        ffn_tern[:, o, k * P:(k + 1) * P], ident_bf[:, :])
                if k % half == half - 1:
                    last.then_inc(ffn_T_done, 1)

            def body(r0, u, first, last):
                r = r0 + u

                def second_product(step, u):
                    pe.wait_ge(aT_moved, step + 1)
                    if not first or u >= PS_RING:
                        pe.wait_ge(y_done, step - PS_RING + 1)
                    for k in range(KH):
                        last_mm = pe.matmul(y_ps[u % PS_RING][:, :], aT[:, u % Q_RING, k * P:(k + 1) * P],
                                            ffnT[:, k, :], start=(k == 0), stop=(k == KH - 1))
                    last_mm.then_inc(y_mm_done, 1)

                def a_transpose(step, u):
                    if first and step == 0:
                        pe.wait_ge(ffn_T_moved, PS_RING)
                    pe.wait_ge(a_int_done, step + 1)
                    if not first or u >= PS_RING:
                        pe.wait_ge(aT_moved, step - PS_RING + 1)
                    for k in range(KH):
                        last_t = pe.transpose(aT_ps[u % PS_RING][:, k * P:(k + 1) * P],
                                              a_int[:, u % Q_RING, k * P:(k + 1) * P], ident_bf[:, :])
                    last_t.then_inc(aT_done, 1)

                _, offset = w_slot(pe, r)
                if not last or u + X_AHEAD < U:
                    pe.wait_ge(x_lo_done, r + X_AHEAD - PS_RING + 1)
                    n = (u + X_AHEAD) % U
                    x_transpose(r + X_AHEAD, n)
                pe.wait_ge(x_lo_done, r + 1)
                if first and u < W_AHEAD:
                    pe.wait_ge(start_lo_done, min(u + 1, 2))
                    pe.wait_ge(pool_w_done, min(u + 1, 2))
                if not first or u >= PS_RING:
                    pe.wait_ge(cond_done, r - PS_RING + 1)
                n = u % XT_RING
                for k in range(KD):
                    x_hi_k = xT_hi[:, n, k * P:(k + 1) * P]
                    x_lo_k = xT_lo[:, n, k * P:(k + 1) * P]
                    w_hi_k = w_hi[:, bass.ds(offset + k * H, H)]
                    w_lo_k = w_lo[:, bass.ds(offset + k * H, H)]
                    ps_cond = cond_ps[u % PS_RING][:, :]
                    pe.matmul(ps_cond, x_hi_k, w_hi_k, start=(k == 0), stop=False)
                    pe.matmul(ps_cond, x_hi_k, w_lo_k, start=False, stop=False)
                    last_mm = pe.matmul(ps_cond, x_lo_k, w_hi_k, start=False, stop=(k == KD - 1))
                last_mm.then_inc(cond_mm_done, 1)
                if not first or u >= 1:
                    a_transpose(r - 1, (u - 1) % U)
                if not first or u >= MM2_BEHIND:
                    second_product(r - MM2_BEHIND, (u - MM2_BEHIND) % U)
                if last and u == U - 1:
                    second_product(r - 1, u - 1)
                    a_transpose(r, u)
                    second_product(r, u)

            over_steps(pe, body)


def kernel(x, itok_B_0_63, L0_cond_W, L0_cond_b, L0_ffn_weight):
    import numpy as np
    import concourse.bacc as bacc
    from concourse.bass_utils import run_bass_kernel_spmd

    nc = bacc.Bacc("TRN2", target_bir_lowering=False, num_devices=1)
    arrays, args = {}, []
    given = {"x": x, "itok": itok_B_0_63, "cond_w": L0_cond_W, "cond_b": L0_cond_b, "ffn_w": L0_ffn_weight}
    for name, a in given.items():
        a = np.ascontiguousarray(a)
        arrays[name] = a
        args.append(nc.dram_tensor(name, a.shape, mybir.dt.from_np(a.dtype), kind="ExternalInput").ap())
    out = nc.dram_tensor("out", x.shape, mybir.dt.float32, kind="ExternalOutput").ap()
    adaln_ffn(nc, *args, out)
    return run_bass_kernel_spmd(nc, [arrays], core_ids=[0]).results[0]["out"]
```
